# Optimizing a Trainium2 kernel written in Bass

```python
import numpy as np
import jax
import jax.numpy as jnp

def _softmax(x, axis=-1):
    return jax.nn.softmax(x, axis=axis)

def _gelu(x):
    return jax.nn.gelu(x, approximate=True)

def _silu(x):
    return jax.nn.silu(x)

def _sigmoid(x):
    return jax.nn.sigmoid(x)

def _layernorm(x, axis=-1, eps=1e-05):
    m = jnp.mean(x, axis=axis, keepdims=True)
    v = jnp.var(x, axis=axis, keepdims=True)
    return (x - m) / jnp.sqrt(v + eps)

def _scatter_add(tgt, idx, src, axis=0):
    return tgt.at[idx].add(src)

def _segment_sum(src, seg, n):
    return jax.ops.segment_sum(src, seg, n)
kernel_name = 'mk_cond_resid_d2_seqx_r2_667f55'

def setup_inputs(seed: int=0):
    np.random.seed(seed)
    _w = jnp.asarray

    def _rec_inputs():
        import jax
        import jax.numpy as jnp
        _rk = jax.random.key(seed)
        x = 0.0001044 + 1 * jax.random.normal(jax.random.fold_in(_rk, 1), (2, 2048, 512), jnp.float32)
        _lenS = 2048 - jax.random.randint(jax.random.fold_in(_rk, 7), (2,), 0, max(1, 2048 // 4) + 1, jnp.int32)
        _lenS2 = 2048 - jax.random.randint(jax.random.fold_in(_rk, 8), (2,), 0, max(1, 2048 // 4) + 1, jnp.int32)
        cond_1024 = 0.00141218 + 0.997886 * jax.random.normal(jax.random.fold_in(_rk, 11), (2, 512), jnp.float32)
        return (x, cond_1024)
    x, cond_1024 = _rec_inputs()

    def _L0_cond_setup():
        import jax, jax.numpy as jnp
        import numpy as np
        B, T, C = (64, 256, 512)
        key = jax.random.key(seed)
        ks = jax.random.split(key, 17)
        s_in = 1.0 / np.sqrt(C)

        def lin(kw, kb, fan_in):
            s = 1.0 / np.sqrt(fan_in)
            W = jax.random.uniform(kw, (C, fan_in), jnp.float32, -s, s)
            b = jax.random.uniform(kb, (C,), jnp.float32, -s, s)
            return (W, b)
        Wxz, bxz = lin(ks[0], ks[1], C)
        Whz, bhz = lin(ks[2], ks[3], C)
        Wxr, bxr = lin(ks[4], ks[5], C)
        Whr, bhr = lin(ks[6], ks[7], C)
        Wxh, bxh = lin(ks[8], ks[9], C)
        Whh, bhh = lin(ks[10], ks[11], C)
        Whq, bhq = lin(ks[12], ks[13], C)
        X = jax.random.normal(ks[14], (B, T, C), jnp.float32)
        h0 = jax.random.normal(ks[15], (B, C), jnp.float32)
        return {'X': X, 'h0': h0, 'Wxz': Wxz, 'bxz': bxz, 'Whz': Whz, 'bhz': bhz, 'Wxr': Wxr, 'bxr': bxr, 'Whr': Whr, 'bhr': bhr, 'Wxh': Wxh, 'bxh': bxh, 'Whh': Whh, 'bhh': bhh, 'Whq': Whq, 'bhq': bhq}
    _L0_cond_all = _L0_cond_setup()
    _L0_cond_in = {k: v for k, v in _L0_cond_all.items() if k in ('Wxz', 'bxz', 'Whz', 'bhz', 'Wxr', 'bxr', 'Whr', 'bhr', 'Wxh', 'bxh', 'Whh', 'bhh', 'Whq', 'bhq')}
    del _L0_cond_all

    def _L1_cond_setup():
        import jax, jax.numpy as jnp
        import numpy as np
        INPUT_DIM = 512
        LATENT_DIM = 512
        key = jax.random.key(seed)
        ks = jax.random.split(key, 8)
        B, T = (64, 256)
        concat_dim = INPUT_DIM + LATENT_DIM
        s = lambda fan_in: 1.0 / np.sqrt(fan_in)
        return {'x': jax.random.normal(ks[0], (B, T, INPUT_DIM), dtype=jnp.float32), 'h0': jax.random.normal(ks[1], (B, LATENT_DIM), dtype=jnp.float32), 'w_W': jax.random.uniform(ks[2], (concat_dim, 2 * LATENT_DIM), jnp.float32, -s(concat_dim), s(concat_dim)), 'w_b': jax.random.uniform(ks[3], (2 * LATENT_DIM,), jnp.float32, -s(concat_dim), s(concat_dim)), 'wx_W': jax.random.uniform(ks[4], (INPUT_DIM, LATENT_DIM), jnp.float32, -s(INPUT_DIM), s(INPUT_DIM)), 'wx_b': jax.random.uniform(ks[5], (LATENT_DIM,), jnp.float32, -s(INPUT_DIM), s(INPUT_DIM)), 'wh_W': jax.random.uniform(ks[6], (LATENT_DIM, LATENT_DIM), jnp.float32, -s(LATENT_DIM), s(LATENT_DIM)), 'wh_b': jax.random.uniform(ks[7], (LATENT_DIM,), jnp.float32, -s(LATENT_DIM), s(LATENT_DIM))}
    _L1_cond_all = _L1_cond_setup()
    _L1_cond_in = {k: v for k, v in _L1_cond_all.items() if k in ('w_W', 'w_b', 'wx_W', 'wx_b', 'wh_W', 'wh_b')}
    del _L1_cond_all
    return {'x': x, 'cond_1024': cond_1024, 'L0_cond_Wxz': _L0_cond_in['Wxz'], 'L0_cond_bxz': _L0_cond_in['bxz'], 'L0_cond_Whz': _L0_cond_in['Whz'], 'L0_cond_bhz': _L0_cond_in['bhz'], 'L0_cond_Wxr': _L0_cond_in['Wxr'], 'L0_cond_bxr': _L0_cond_in['bxr'], 'L0_cond_Whr': _L0_cond_in['Whr'], 'L0_cond_bhr': _L0_cond_in['bhr'], 'L0_cond_Wxh': _L0_cond_in['Wxh'], 'L0_cond_bxh': _L0_cond_in['bxh'], 'L0_cond_Whh': _L0_cond_in['Whh'], 'L0_cond_bhh': _L0_cond_in['bhh'], 'L0_cond_Whq': _L0_cond_in['Whq'], 'L0_cond_bhq': _L0_cond_in['bhq'], 'L1_cond_w_W': _L1_cond_in['w_W'], 'L1_cond_w_b': _L1_cond_in['w_b'], 'L1_cond_wx_W': _L1_cond_in['wx_W'], 'L1_cond_wx_b': _L1_cond_in['wx_b'], 'L1_cond_wh_W': _L1_cond_in['wh_W'], 'L1_cond_wh_b': _L1_cond_in['wh_b']}

def reference(x, cond_1024, L0_cond_Wxz, L0_cond_bxz, L0_cond_Whz, L0_cond_bhz, L0_cond_Wxr, L0_cond_bxr, L0_cond_Whr, L0_cond_bhr, L0_cond_Wxh, L0_cond_bxh, L0_cond_Whh, L0_cond_bhh, L0_cond_Whq, L0_cond_bhq, L1_cond_w_W, L1_cond_w_b, L1_cond_wx_W, L1_cond_wx_b, L1_cond_wh_W, L1_cond_wh_b):
    import jax
    import jax.numpy as jnp

    def _L0_cond_ref(X, h0, Wxz, bxz, Whz, bhz, Wxr, bxr, Whr, bhr, Wxh, bxh, Whh, bhh, Whq, bhq):
        import jax, jax.numpy as jnp
        import numpy as np
        B, T, C = (64, 256, 512)
        Xz = jnp.einsum('btc,hc->tbh', X, Wxz) + bxz
        Xr = jnp.einsum('btc,hc->tbh', X, Wxr) + bxr
        Xh = jnp.einsum('btc,hc->tbh', X, Wxh) + bxh

        def step(H, xs):
            xz, xr, xh = xs
            Z = jax.nn.sigmoid(xz + H @ Whz.T + bhz)
            R = jax.nn.sigmoid(xr + H @ Whr.T + bhr)
            H_tilda = jnp.tanh(xh + R * H @ Whh.T + bhh)
            H_new = Z * H + (1.0 - Z) * H_tilda
            Y = H_new @ Whq.T + bhq
            return (H_new, Y)
        _, Ys = jax.lax.scan(step, h0, (Xz, Xr, Xh))
        return jnp.transpose(Ys, (1, 0, 2))

    def _L1_cond_ref(x, h0, w_W, w_b, wx_W, wx_b, wh_W, wh_b):
        import jax, jax.numpy as jnp
        import numpy as np
        INPUT_DIM = 512
        LATENT_DIM = 512
        xT = jnp.swapaxes(x, 0, 1)

        def step(h, x_t):
            fused = jax.nn.sigmoid(jnp.concatenate([x_t, h], axis=-1) @ w_W + w_b)
            hidden_state, output_state = jnp.split(fused, 2, axis=-1)
            memory_state = x_t @ wx_W + wx_b + hidden_state * (h @ wh_W + wh_b)
            h_new = output_state * h + (1.0 - output_state) * jnp.tanh(memory_state)
            return (h_new, h_new)
        _, hs = jax.lax.scan(step, h0, xT)
        return jnp.swapaxes(hs, 0, 1)
    x = x + _L0_cond_ref(x, cond_1024, L0_cond_Wxz, L0_cond_bxz, L0_cond_Whz, L0_cond_bhz, L0_cond_Wxr, L0_cond_bxr, L0_cond_Whr, L0_cond_bhr, L0_cond_Wxh, L0_cond_bxh, L0_cond_Whh, L0_cond_bhh, L0_cond_Whq, L0_cond_bhq)
    x = x + _L1_cond_ref(x, cond_1024, L1_cond_w_W, L1_cond_w_b, L1_cond_wx_W, L1_cond_wx_b, L1_cond_wh_W, L1_cond_wh_b)
    return x

_drawn_inputs = setup_inputs


def setup_inputs(seed=0):
    import zlib

    import numpy as np

    out = dict(_drawn_inputs(seed))
    spreads = {}
    factors = {'cond_1024': 3.557,
     'L0_cond_bxz': 24.041,
     'L0_cond_Whz': 4.227,
     'L0_cond_bhz': 26.163,
     'L0_cond_Wxr': 8.0,
     'L0_cond_bxr': 200.0,
     'L0_cond_Whr': 8.0,
     'L0_cond_bhr': 200.0,
     'L0_cond_bxh': 4.403,
     'L0_cond_bhh': 4.351,
     'L1_cond_w_b': 25.599,
     'L1_cond_wx_b': 2.814,
     'L1_cond_wh_b': 5.718}
    for name, (base, spread) in spreads.items():
        noise = np.random.default_rng([zlib.crc32(name.encode()), seed]).standard_normal(out[name].shape)
        drawn = base * np.exp(spread * noise) if base else spread * noise
        out[name] = jnp.asarray(drawn.astype(out[name].dtype))
    for name, factor in factors.items():
        out[name] = (out[name] * factor).astype(out[name].dtype)
    return out
```

```python
import numpy as np
from contextlib import ExitStack

import concourse.bass as bass
from concourse import mybir

P = 128
Q = 32
G = P // Q


def gated_recurrences(nc: bass.Bass, x_t, h_init, w_rz, w_h, w_fow, w_x0, w_y, w_x1, bias, out_t):
    fp32 = mybir.dt.float32
    ALU = mybir.AluOpType
    ACT = mybir.ActivationFunctionType

    CHUNKS, _, J, TS, B = x_t.shape
    JB = J * B
    N = TS * B
    UNROLL = 8
    assert TS % UNROLL == 0 and CHUNKS >= 2

    ctx = ExitStack()
    with ctx:
        def sb(name, shape):
            return ctx.enter_context(nc.sbuf_tensor(name, shape, fp32))

        def ps(name, shape):
            return ctx.enter_context(nc.psum_tensor(name, shape, fp32))

        def sem(name):
            return ctx.enter_context(nc.semaphore(name))

        wrz = sb("wrz", [P, J, G, 2 * P])
        wh = sb("wh", [P, J, G, P])
        wfow = sb("wfow", [P, J, G, 3 * P])
        wx0 = sb("wx0", [P, J, 3, J, P])
        wy = sb("wy", [P, J, 1, J, P])
        wx1 = sb("wx1", [P, J, 3, J, P])
        biases = sb("biases", [P, 11, J])
        bias0 = sb("bias0", [P, 3, J])
        hidden_bias = sb("hidden_bias", [P, J, B])

        h_first = sb("h_first", [P, J, B])

        x_in = sb("x_in", [P, J, N])
        x_res = sb("x_res", [P, J, N])
        x1 = sb("x1", [P, J, N])
        h0_seq = sb("h0_seq", [P, J, N])
        result = sb("result", [P, J, N])
        proj0 = sb("proj0", [P, TS, 3 * JB])
        proj1 = sb("proj1", [P, TS, 3 * JB])

        h0 = sb("h0", [P, J, B])
        rz_t = sb("rz_t", [P, 2 * P])
        h_t = sb("h_t", [P, P])
        r_pre = sb("r_pre", [P, J, B])
        z_pre = sb("z_pre", [P, J, B])
        h_pre = sb("h_pre", [P, J, B])
        r = sb("r", [P, J, B])
        z = sb("z", [P, J, B])
        z_not = sb("z_not", [P, J, B])
        rh = sb("rh", [P, J, B])
        cand0 = sb("cand0", [P, J, B])
        kept0 = sb("kept0", [P, J, B])
        new0 = sb("new0", [P, J, B])

        h1 = sb("h1", [P, J, B])
        fow_t = sb("fow_t", [P, 3 * P])
        fo_pre = sb("fo_pre", [P, 2 * J, B])
        fo = sb("fo", [P, 2 * J, B])
        o_not = sb("o_not", [P, J, B])
        hid = sb("hid", [P, J, B])
        gated = sb("gated", [P, J, B])
        mem = sb("mem", [P, J, B])
        cand1 = sb("cand1", [P, J, B])
        kept1 = sb("kept1", [P, J, B])
        new1 = sb("new1", [P, J, B])

        bank_rz = ps("bank_rz", [P, 512])
        bank_h = ps("bank_h", [P, 512])
        bank_fow = ps("bank_fow", [P, 512])
        bank_chunk = [ps(f"bank_chunk{n}", [P, 512]) for n in range(5)]

        consts_in = sem("consts_in")
        x_in_loaded = sem("x_in_loaded")
        x_res_loaded = sem("x_res_loaded")
        result_free = sem("result_free")
        banks_cleared, biases_made = sem("banks_cleared"), sem("biases_made")
        y_mm, x1_ready = sem("y_mm"), sem("x1_ready")
        p0_mm, p0_ready = sem("p0_mm"), sem("p0_ready")
        p1_mm, p1_ready = sem("p1_mm"), sem("p1_ready")
        rz_mm, h_mm = sem("rz_mm"), sem("h_mm")
        r_turned, r_summed, r_done = sem("r_turned"), sem("r_summed"), sem("r_done")
        z_turned, z_summed, z_done = sem("z_turned"), sem("z_summed"), sem("z_done")
        rh_done = sem("rh_done")
        h_turned, h_summed, cand0_done = sem("h_turned"), sem("h_summed"), sem("cand0_done")
        new0_done, h0_done = sem("new0_done"), sem("h0_done")
        h0_kept = sem("h0_kept")
        fow_mm, fo_turned, fo_summed = sem("fow_mm"), sem("fo_turned"), sem("fo_summed")
        w_turned = sem("w_turned")
        fo_done = sem("fo_done")
        hid_done, gated_done, mem_done = sem("hid_done"), sem("gated_done"), sem("mem_done")
        cand1_done, kept1_done, new1_done = sem("cand1_done"), sem("kept1_done"), sem("new1_done")
        h1_done, result_done = sem("h1_done"), sem("result_done")

        WEIGHTS = [(wx0, w_x0), (wrz, w_rz), (wh, w_h), (wy, w_y), (wx1, w_x1), (wfow, w_fow)]
        weights_in = [sem(f"{n}_in") for n in ("wx0", "wrz", "wh", "wy", "wx1", "wfow")]

        block = ctx.enter_context(nc.Block())

        def steps(eng, layer0, layer1, body, needs=()):
            with eng.Fori(0, TS // UNROLL) as i:
                for u in range(UNROLL):
                    for semaphore, count in needs if u == 0 else ():
                        eng.wait_ge(semaphore, count)
                    t = i * UNROLL + u
                    body(t, *(None if c is None else eng.snap(c * TS + t) for c in (layer0, layer1)))

        def turned(t, first, count):
            return t[:, first * Q:(first + count) * Q].rearrange("p (j c) -> p j c", c=Q)[:, :, 0:B]

        def columns(t, step):
            return t[:, :, bass.ds(step * B, B)]

        def proj(t, step, first, count):
            return t[:, bass.ds(step, 1), first * JB:(first + count) * JB].rearrange("p a (j b) -> p (a j) b", b=B)

        @block.sync
        def _(eng):
            eng.dma_start(x_in[:], x_t[0].rearrange("p j t b -> p j (t b)")).then_inc(x_in_loaded, 16)
            eng.dma_start(biases[:], bias).then_inc(consts_in, 16)
            eng.dma_start(h_first[:], h_init).then_inc(consts_in, 16)
            eng.sem_inc(result_free, 16)
            for (to, of), there in zip(WEIGHTS, weights_in):
                eng.dma_start(to[:], of).then_inc(there, 16)

            def next_in(c):
                eng.wait_ge(p0_mm, 3 * (c + 1))
                eng.dma_start(x_in[:], x_t[bass.ds(c + 1, 1)].rearrange("a p j t b -> p (a j) (t b)")).then_inc(x_in_loaded, 16)

            def next_res(c):
                eng.wait_ge(x1_ready, c * 1)
                eng.dma_start(x_res[:], x_t[bass.ds(c, 1)].rearrange("a p j t b -> p (a j) (t b)")).then_inc(x_res_loaded, 16)

            def store(c):
                eng.wait_ge(result_done, (c + 1) * TS + 1)
                eng.dma_start(out_t[bass.ds(c, 1)].rearrange("a p j t b -> p (a j) (t b)"), result[:]).then_inc(result_free, 16)

            next_in(0)
            eng.dma_start(x_res[:], x_t[0].rearrange("p j t b -> p j (t b)")).then_inc(x_res_loaded, 16)
            with eng.Fori(1, CHUNKS - 1) as c:
                next_in(c)
                next_res(c)
                store(c - 1)
            next_res(CHUNKS - 1)
            store(CHUNKS - 2)
            store(CHUNKS - 1)
            eng.wait_ge(result_free, 16 * CHUNKS + 16)

        @block.tensor
        def _(eng):
            def chunk_product(w, m, of, bank):
                for j in range(J):
                    for k in range(J):
                        last = nc.tensor.matmul(bank[:, j * N:(j + 1) * N], w[:, k, m, j, :], of[:, k, :],
                                                start=(k == 0), stop=(k == J - 1))
                return last

            def y_product(c):
                eng.wait_ge(h0_kept, (c + 1) * TS + 1)
                chunk_product(wy, 0, h0_seq, bank_chunk[0]).then_inc(y_mm, 1)

            def proj0_products(c):
                eng.wait_ge(x_in_loaded, (c + 1) * 16)
                for m in range(3):
                    chunk_product(wx0, m, x_in, bank_chunk[1 + m]).then_inc(p0_mm, 1)

            def proj1_products(c):
                eng.wait_ge(x1_ready, c + 1)
                for m in range(3):
                    if m == 2:
                        eng.wait_ge(p0_ready, 3 * c + 4)
                    chunk_product(wx1, m, x1, bank_chunk[(4, 0, 1)[m]]).then_inc(p1_mm, 1)

            def recurrent(w, state, bank, n, ks):
                for k in ks:
                    for g in range(G):
                        last = nc.tensor.matmul(bank[Q * g:Q * g + B, 0:n], state[:, k, :], w[:, k, g, :],
                                                start=(k == 0), stop=(k == J - 1), skip_group_check=True)
                return last

            def step(t, s0, s1):
                if s0 is not None:
                    eng.wait_ge(h0_done, s0 + 1)
                    recurrent(wrz, h0, bank_rz, 2 * P, range(J)).then_inc(rz_mm, 1)
                if s1 is not None:
                    eng.wait_ge(h1_done, s1 + 1)
                    recurrent(wfow, h1, bank_fow, 3 * P, range(J // 2))
                if s0 is not None:
                    eng.wait_ge(rh_done, s0 + 1)
                    recurrent(wh, rh, bank_h, P, range(J)).then_inc(h_mm, 1)
                if s1 is not None:
                    recurrent(wfow, h1, bank_fow, 3 * P, range(J // 2, J)).then_inc(fow_mm, 1)

            eng.wait_ge(weights_in[0], 16)
            eng.wait_ge(banks_cleared, 3)
            proj0_products(0)
            for there in weights_in[1:3]:
                eng.wait_ge(there, 16)
            steps(eng, 0, None, step)
            for there in weights_in[3:]:
                eng.wait_ge(there, 16)
            with eng.Fori(1, CHUNKS) as c:
                y_product(c - 1)
                proj0_products(c)
                proj1_products(c - 1)
                steps(eng, c, c - 1, step)
            y_product(CHUNKS - 1)
            eng.wait_ge(x1_ready, CHUNKS)
            for m in range(3):
                chunk_product(wx1, m, x1, bank_chunk[(4, 0, 1)[m]]).then_inc(p1_mm, 1)
            steps(eng, None, CHUNKS - 1, step)

        @block.scalar
        def _(eng):
            def step(t, s0, s1):
                if s0 is not None:
                    eng.wait_ge(r_summed, s0 + 1)
                    nc.scalar.activation(r[:], r_pre[:], ACT.Sigmoid).then_inc(r_done, 1)
                    eng.wait_ge(z_summed, s0 + 1)
                    nc.scalar.activation(z[:], z_pre[:], ACT.Sigmoid)
                    nc.scalar.activation(z_not[:], z_pre[:], ACT.Sigmoid, scale=-1.0).then_inc(z_done, 1)
                    eng.wait_ge(h_summed, s0 + 1)
                    nc.scalar.activation(cand0[:], h_pre[:], ACT.Tanh).then_inc(cand0_done, 1)
                if s1 is not None:
                    eng.wait_ge(fo_summed, s1 + 1)
                    nc.scalar.activation(fo[:], fo_pre[:], ACT.Sigmoid).then_inc(fo_done, 1)
                    nc.scalar.activation(o_not[:], fo_pre[:, J:2 * J, :], ACT.Sigmoid, scale=-1.0)
                    eng.wait_ge(mem_done, s1 + 1)
                    nc.scalar.activation(cand1[:], mem[:], ACT.Tanh).then_inc(cand1_done, 1)

            steps(eng, 0, None, step)
            with eng.Fori(1, CHUNKS) as c:
                steps(eng, c, c - 1, step)
            steps(eng, None, CHUNKS - 1, step)

        @block.vector
        def _(eng):
            def spread(column, name_j):
                return column.unsqueeze(2).to_broadcast([P, J, name_j])

            def set_up():
                for n, bank in enumerate((bank_rz, bank_h, bank_fow)):
                    nc.vector.memset(bank[:], 0.0).then_inc(banks_cleared, 1)
                eng.wait_ge(consts_in, 32)
                nc.vector.tensor_tensor(bias0[:], biases[:, 0:3, :], biases[:, 3:6, :], ALU.add).then_inc(biases_made, 1)
                for b in range(B):
                    nc.vector.tensor_copy(hidden_bias[:, :, b], biases[:, 10, :]).then_inc(biases_made, 1)
                eng.wait_ge(biases_made, 1 + B)
                nc.vector.tensor_copy(h0[:], h_first[:]).then_inc(h0_done, 1)
                nc.vector.tensor_copy(h1[:], h_first[:]).then_inc(h1_done, 1)

            def into_steps(t, m, bank, column):
                for b in range(B):
                    to = t[:, :, m * JB:(m + 1) * JB].rearrange("p t (j b) -> p b j t", b=B)[:, b]
                    of = bank[:, 0:J * N].rearrange("p (j t b) -> p b j t", j=J, b=B)[:, b]
                    last = nc.vector.tensor_tensor(to, of, column.unsqueeze(2).to_broadcast([P, J, TS]), ALU.add)
                return last

            def make_x1(c):
                eng.wait_ge(y_mm, c + 1)
                eng.wait_ge(x_res_loaded, (c + 1) * 16)
                for j in range(J):
                    last = nc.vector.scalar_tensor_tensor(out=x1[:, j, :], in0=bank_chunk[0][:, j * N:(j + 1) * N],
                                                          scalar=biases[:, 6, j:j + 1], in1=x_res[:, j, :],
                                                          op0=ALU.add, op1=ALU.add)
                last.then_inc(x1_ready, 1)

            def take_proj0(c):
                for m in range(3):
                    eng.wait_ge(p0_mm, 3 * c + m + 1)
                    into_steps(proj0, m, bank_chunk[1 + m], bias0[:, m, :]).then_inc(p0_ready, 1)

            def take_proj1(c):
                for m in range(3):
                    eng.wait_ge(p1_mm, 3 * c + m + 1)
                    into_steps(proj1, m, bank_chunk[(4, 0, 1)[m]], biases[:, 7 + m, :]).then_inc(p1_ready, 1)

            def step(t, s0, s1):
                if s0 is not None:
                    r_in, z_in, h_in = (proj(proj0, t, m, 1) for m in range(3))
                    for ap in (r_in, z_in, h_in):
                        eng.lower_ap(ap)
                if s1 is not None:
                    fo_in, w_in = proj(proj1, t, 0, 2), proj(proj1, t, 2, 1)
                    for ap in (fo_in, w_in):
                        eng.lower_ap(ap)
                if s0 is not None:
                    eng.wait_ge(rz_mm, s0 + 1)
                    nc.vector.transpose(rz_t[:, 0:P], bank_rz[:, 0:P]).then_inc(r_turned, 1)
                    eng.wait_ge(r_turned, s0 + 1)
                    nc.vector.tensor_tensor(r_pre[:], turned(rz_t, 0, J), r_in, ALU.add).then_inc(r_summed, 1)
                    nc.vector.transpose(rz_t[:, P:2 * P], bank_rz[:, P:2 * P]).then_inc(z_turned, 1)
                    eng.wait_ge(r_done, s0 + 1)
                    nc.vector.tensor_tensor(rh[:], r[:], h0[:], ALU.mult).then_inc(rh_done, 1)
                    eng.wait_ge(z_turned, s0 + 1)
                    nc.vector.tensor_tensor(z_pre[:], turned(rz_t, J, J), z_in, ALU.add).then_inc(z_summed, 1)
                    eng.wait_ge(z_done, s0 + 1)
                    eng.wait_ge(h0_kept, s0 + 1)
                    nc.vector.tensor_tensor(kept0[:], z[:], h0[:], ALU.mult)
                    eng.wait_ge(h_mm, s0 + 1)
                    nc.vector.transpose(h_t[:], bank_h[:, 0:P]).then_inc(h_turned, 1)
                    eng.wait_ge(h_turned, s0 + 1)
                    nc.vector.tensor_tensor(h_pre[:], turned(h_t, 0, J), h_in, ALU.add).then_inc(h_summed, 1)
                    eng.wait_ge(cand0_done, s0 + 1)
                    nc.vector.tensor_tensor(new0[:], z_not[:], cand0[:], ALU.mult).then_inc(new0_done, 1)
                    eng.wait_ge(new0_done, s0 + 1)
                    nc.vector.tensor_tensor(h0[:], new0[:], kept0[:], ALU.add).then_inc(h0_done, 1)
                if s1 is not None:
                    eng.wait_ge(fow_mm, s1 + 1)
                    nc.vector.transpose(fow_t[:, 0:2 * P], bank_fow[:, 0:2 * P]).then_inc(fo_turned, 1)
                    eng.wait_ge(fo_turned, s1 + 1)
                    nc.vector.tensor_tensor(fo_pre[:], turned(fow_t, 0, 2 * J), fo_in, ALU.add).then_inc(fo_summed, 1)
                    nc.vector.transpose(fow_t[:, 2 * P:3 * P], bank_fow[:, 2 * P:3 * P]).then_inc(w_turned, 1)
                    eng.wait_ge(w_turned, s1 + 1)
                    nc.vector.tensor_tensor(hid[:], turned(fow_t, 2 * J, J), hidden_bias[:], ALU.add).then_inc(hid_done, 1)
                    eng.wait_ge(fo_done, s1 + 1)
                    eng.wait_ge(hid_done, s1 + 1)
                    nc.vector.tensor_tensor(gated[:], fo[:, 0:J, :], hid[:], ALU.mult).then_inc(gated_done, 1)
                    eng.wait_ge(gated_done, s1 + 1)
                    nc.vector.tensor_tensor(mem[:], gated[:], w_in, ALU.add).then_inc(mem_done, 1)
                    eng.wait_ge(result_done, s1 + 1)
                    nc.vector.tensor_tensor(kept1[:], fo[:, J:2 * J, :], h1[:], ALU.mult).then_inc(kept1_done, 1)
                    eng.wait_ge(cand1_done, s1 + 1)
                    nc.vector.tensor_tensor(new1[:], o_not[:], cand1[:], ALU.mult).then_inc(new1_done, 1)
                    eng.wait_ge(new1_done, s1 + 1)
                    eng.wait_ge(kept1_done, s1 + 1)
                    nc.vector.tensor_tensor(h1[:], new1[:], kept1[:], ALU.add).then_inc(h1_done, 1)

            set_up()
            take_proj0(0)
            eng.wait_ge(p0_ready, 3)
            steps(eng, 0, None, step)
            with eng.Fori(1, CHUNKS) as c:
                eng.wait_ge(result_done, (c - 1) * TS + 1)
                make_x1(c - 1)
                take_proj0(c)
                take_proj1(c - 1)
                steps(eng, c, c - 1, step, [(p0_ready, 3 * c + 3), (p1_ready, 3 * c)])
            eng.wait_ge(result_done, (CHUNKS - 1) * TS + 1)
            make_x1(CHUNKS - 1)
            take_proj1(CHUNKS - 1)
            eng.wait_ge(p1_ready, 3 * CHUNKS)
            steps(eng, None, CHUNKS - 1, step)

        @block.gpsimd
        def _(eng):
            def step(t, s0, s1):
                if s0 is not None:
                    eng.wait_ge(h0_done, s0 + 2)
                    nc.gpsimd.tensor_copy(columns(h0_seq, t), h0[:]).then_inc(h0_kept, 1)
                if s1 is not None:
                    eng.wait_ge(h1_done, s1 + 2)
                    nc.gpsimd.tensor_tensor(columns(result, t), columns(x1, t), h1[:], ALU.add).then_inc(result_done, 1)

            eng.sem_inc(h0_kept, 1)
            eng.sem_inc(result_done, 1)
            steps(eng, 0, None, step)
            with eng.Fori(1, CHUNKS) as c:
                steps(eng, c, c - 1, step, [(y_mm, c), (result_free, c * 16)])
            eng.wait_ge(result_free, CHUNKS * 16)
            steps(eng, None, CHUNKS - 1, step)


TS = 64


def kernel(x, cond_1024, L0_cond_Wxz, L0_cond_bxz, L0_cond_Whz, L0_cond_bhz, L0_cond_Wxr, L0_cond_bxr,
           L0_cond_Whr, L0_cond_bhr, L0_cond_Wxh, L0_cond_bxh, L0_cond_Whh, L0_cond_bhh, L0_cond_Whq,
           L0_cond_bhq, L1_cond_w_W, L1_cond_w_b, L1_cond_wx_W, L1_cond_wx_b, L1_cond_wh_W, L1_cond_wh_b):
    import concourse.bacc as bacc
    from concourse.bass_utils import run_bass_kernel_spmd

    x = np.asarray(x)
    Bt, T, C = x.shape
    J = C // P

    def features(a, axis):
        a = np.moveaxis(np.asarray(a), axis, 0)
        rest = a.shape[1:]
        a = a.reshape(G, J, Q, *rest).swapaxes(1, 2).reshape(P, J, *rest)
        return a

    def streamed(*mats):
        rows = [features(m, 0).reshape(P, J, G, P) for m in mats]
        return np.ascontiguousarray(np.concatenate(rows, axis=3))

    def stationary(*mats):
        out = []
        for m in mats:
            a = features(m, 0)
            a = features(a, 2)
            out.append(a.transpose(2, 3, 1, 0))
        return np.ascontiguousarray(np.stack(out, axis=2))

    w_W, w_b = np.asarray(L1_cond_w_W), np.asarray(L1_cond_w_b)
    t = [np.asarray(m).T for m in (L0_cond_Whr, L0_cond_Whz, L0_cond_Whh, L0_cond_Wxr, L0_cond_Wxz, L0_cond_Wxh, L0_cond_Whq)]
    bias = [L0_cond_bxr, L0_cond_bxz, L0_cond_bxh, L0_cond_bhr, L0_cond_bhz, L0_cond_bhh, L0_cond_bhq,
            w_b[:C], w_b[C:], L1_cond_wx_b, L1_cond_wh_b]
    arrays = {
        "x_t": np.ascontiguousarray(features(x, 2).reshape(P, J, Bt, T // TS, TS).transpose(3, 0, 1, 4, 2)),
        "h_init": np.ascontiguousarray(features(cond_1024, 1)),
        "w_rz": streamed(t[0], t[1]),
        "w_h": streamed(t[2]),
        "w_fow": streamed(w_W[C:, :C], w_W[C:, C:], np.asarray(L1_cond_wh_W)),
        "w_x0": stationary(t[3], t[4], t[5]),
        "w_y": stationary(t[6]),
        "w_x1": stationary(w_W[:C, :C], w_W[:C, C:], np.asarray(L1_cond_wx_W)),
        "bias": np.ascontiguousarray(np.stack([features(b, 0) for b in bias], axis=1)),
    }
    nc = bacc.Bacc("TRN2", target_bir_lowering=False, num_devices=1)
    args = [nc.dram_tensor(n, a.shape, mybir.dt.from_np(a.dtype), kind="ExternalInput").ap() for n, a in arrays.items()]
    out = nc.dram_tensor("out_t", arrays["x_t"].shape, mybir.dt.float32, kind="ExternalOutput").ap()
    gated_recurrences(nc, *args, out)
    r = run_bass_kernel_spmd(nc, [arrays], core_ids=[0])
    got = r.results[0]["out_t"]
    got = got.transpose(4, 0, 3, 1, 2).reshape(Bt, T, G, Q, J)
    return np.ascontiguousarray(got.transpose(0, 1, 2, 4, 3).reshape(Bt, T, C))
```

```python
import numpy as np
from contextlib import ExitStack

import concourse.bass as bass
from concourse import mybir

P = 128
Q = 32
G = P // Q


def gated_recurrences(nc: bass.Bass, x_t, h_init, w_x0, w_rz, w_h, w_y, w_x1, w_fow, bias, out_t):
    fp32 = mybir.dt.float32
    ALU = mybir.AluOpType
    ACT = mybir.ActivationFunctionType

    CHUNKS, _, J, TS, B = x_t.shape
    JB = J * B
    assert TS * B == Q and J * Q == P and CHUNKS >= 5

    Y_PRODUCTS = {0: 6, 1: 6, 2: 4}
    P0_PRODUCTS = {2: 1, 3: 3, 4: 2, 5: 3, 6: 2, 7: 3, 8: 2}
    P1_PRODUCTS = {9: 3, 10: 2, 11: 2, 12: 3, 13: 2, 14: 2, 15: 2}
    FOW_FIRST = 6
    assert all(sum(n.values()) == J * G for n in (Y_PRODUCTS, P0_PRODUCTS, P1_PRODUCTS))
    Y_TURN, P0_TURN, P1_TURN = 3, 9, 15
    X1_STEP = 4

    ctx = ExitStack()
    with ctx:
        def sb(name, shape):
            return ctx.enter_context(nc.sbuf_tensor(name, shape, fp32))

        def ps(name):
            return ctx.enter_context(nc.psum_tensor(name, [P, 512], fp32))

        def sem(name):
            return ctx.enter_context(nc.semaphore(name))

        wx0 = sb("wx0", [P, J, G, 3 * P])
        wrz = sb("wrz", [P, J, G, 2 * P])
        wh = sb("wh", [P, J, G, P])
        wy = sb("wy", [P, J, G, P])
        wx1 = sb("wx1", [P, J, G, 3 * P])
        wfow = sb("wfow", [P, J, G, 3 * P])
        biases = sb("biases", [P, 11, J])
        gate_bias0 = sb("gate_bias0", [P, 3, J])
        chunk_bias0 = sb("chunk_bias0", [P, 3 * J, Q])
        chunk_bias1 = sb("chunk_bias1", [P, 3 * J, Q])
        chunk_bias_y = sb("chunk_bias_y", [P, J, Q])
        hidden_bias = sb("hidden_bias", [P, J, B])
        h_first = sb("h_first", [P, J, B])

        x_in = sb("x_in", [P, J, Q])
        x_res = sb("x_res", [P, J, Q])
        h0_seq = sb("h0_seq", [P, J, Q])
        h0_last = sb("h0_last", [P, J, Q])
        y_t = sb("y_t", [P, J, Q])
        y_res = sb("y_res", [P, J, Q])
        x1 = sb("x1", [P, J, Q])
        x1_here = sb("x1_here", [P, J, Q])
        result = sb("result", [P, J, Q])
        next0 = sb("next0", [P, 3 * J, Q])
        next1 = sb("next1", [P, 3 * J, Q])
        proj0 = sb("proj0", [P, 3 * J, Q])
        proj1 = sb("proj1", [P, 3 * J, Q])

        h0 = sb("h0", [P, J, B])
        rz_t = sb("rz_t", [P, 2 * J, Q])
        h_t = sb("h_t", [P, J, Q])
        r_pre = sb("r_pre", [P, J, B])
        z_pre = sb("z_pre", [P, J, B])
        h_pre = sb("h_pre", [P, J, B])
        r = sb("r", [P, J, B])
        z = sb("z", [P, J, B])
        rh = sb("rh", [P, J, B])
        cand0 = sb("cand0", [P, J, B])
        kept0 = sb("kept0", [P, J, B])
        new0 = sb("new0", [P, J, B])

        h1 = sb("h1", [P, J, B])
        fow_t = sb("fow_t", [P, 3 * J, Q])
        f_pre = sb("f_pre", [P, J, B])
        o_pre = sb("o_pre", [P, J, B])
        f = sb("f", [P, J, B])
        o = sb("o", [P, J, B])
        hid = sb("hid", [P, J, B])
        gated = sb("gated", [P, J, B])
        mem = sb("mem", [P, J, B])
        cand1 = sb("cand1", [P, J, B])
        kept1 = sb("kept1", [P, J, B])
        new1 = sb("new1", [P, J, B])

        bank_rz, bank_h, bank_fow = ps("bank_rz"), ps("bank_h"), ps("bank_fow")
        bank_y, bank_p0, bank_p1 = ps("bank_y"), ps("bank_p0"), ps("bank_p1")

        consts_in = sem("consts_in")
        banks_cleared, biases_made = sem("banks_cleared"), sem("biases_made")
        x_in_loaded, x_res_loaded = sem("x_in_loaded"), sem("x_res_loaded")
        result_free = sem("result_free")
        y_mm, y_turned, y_res_done, x1_ready = sem("y_mm"), sem("y_turned"), sem("y_res_done"), sem("x1_ready")
        p0_mm, p0_turned, proj0_ready = sem("p0_mm"), sem("p0_turned"), sem("proj0_ready")
        p1_mm, p1_turned, proj1_ready = sem("p1_mm"), sem("p1_turned"), sem("proj1_ready")
        h0_last_ready, x1_here_ready = sem("h0_last_ready"), sem("x1_here_ready")
        rz_mm, h_mm = sem("rz_mm"), sem("h_mm")
        r_turned, r_summed, r_done = sem("r_turned"), sem("r_summed"), sem("r_done")
        z_turned, z_summed, z_done = sem("z_turned"), sem("z_summed"), sem("z_done")
        rh_done = sem("rh_done")
        h_turned, h_summed, cand0_done = sem("h_turned"), sem("h_summed"), sem("cand0_done")
        new0_done, h0_done, h0_kept = sem("new0_done"), sem("h0_done"), sem("h0_kept")
        fow_mm = sem("fow_mm")
        f_turned, f_summed, f_done = sem("f_turned"), sem("f_summed"), sem("f_done")
        o_turned, o_summed, o_done = sem("o_turned"), sem("o_summed"), sem("o_done")
        w_turned = sem("w_turned")
        hid_done, gated_done, mem_done = sem("hid_done"), sem("gated_done"), sem("mem_done")
        cand1_done, kept1_done, new1_done = sem("cand1_done"), sem("kept1_done"), sem("new1_done")
        h1_done, result_done = sem("h1_done"), sem("result_done")

        WEIGHTS = [(wx0, w_x0), (wrz, w_rz), (wh, w_h), (wy, w_y), (wx1, w_x1), (wfow, w_fow)]
        weights_in = [sem(f"{n}_in") for n in ("wx0", "wrz", "wh", "wy", "wx1", "wfow")]

        block = ctx.enter_context(nc.Block())

        def iterations(eng, body):
            body(0, True, False, False, True)
            body(1, True, False, True, True)
            with eng.Fori(2, CHUNKS) as c:
                body(c, True, True, True, True)
            body(CHUNKS, False, True, True, False)
            body(CHUNKS + 1, False, True, False, False)

        def turned(t, first, count):
            return t[:, first:first + count, 0:B]

        def columns(t, u, first=0, count=J):
            return t[:, first:first + count, u * B:(u + 1) * B]

        @block.sync
        def _(eng):
            def chunk_of(t, c):
                return t[bass.ds(c, 1)].rearrange("a p j t b -> p (a j) (t b)")

            eng.dma_start(x_in[:], chunk_of(x_t, 0)).then_inc(x_in_loaded, 16)
            eng.dma_start(biases[:], bias).then_inc(consts_in, 16)
            eng.dma_start(h_first[:], h_init).then_inc(consts_in, 16)
            eng.sem_inc(result_free, 16)
            for (to, of), there in zip(WEIGHTS, weights_in):
                eng.dma_start(to[:], of).then_inc(there, 16)
            eng.dma_start(x_res[:], chunk_of(x_t, 0)).then_inc(x_res_loaded, 16)

            def load_in(c, of):
                eng.wait_ge(p0_mm, c)
                eng.dma_start(x_in[:], chunk_of(x_t, of)).then_inc(x_in_loaded, 16)

            def load_res(c):
                eng.wait_ge(x1_ready, c)
                eng.dma_start(x_res[:], chunk_of(x_t, c)).then_inc(x_res_loaded, 16)

            def store(c):
                eng.wait_ge(result_done, (c + 1) * TS + 1)
                eng.dma_start(chunk_of(out_t, c), result[:]).then_inc(result_free, 16)

            load_in(1, 1)
            load_in(2, 2)
            load_res(1)
            load_in(3, 3)
            with eng.Fori(2, CHUNKS - 2) as c:
                load_res(c)
                load_in(c + 2, c + 2)
                store(c - 2)
            load_res(CHUNKS - 2)
            load_in(CHUNKS, CHUNKS - 1)
            store(CHUNKS - 4)
            load_res(CHUNKS - 1)
            for c in range(CHUNKS - 3, CHUNKS):
                store(c)
            eng.wait_ge(result_free, 16 * CHUNKS + 16)
            eng.wait_ge(x_in_loaded, 16 * CHUNKS + 16)

        @block.tensor
        def _(eng):
            BLOCKS = [(k, g) for k in range(J) for g in range(G)]

            def product(w, state, bank, blocks):
                rows, n = state.shape[2], w.shape[3]
                for k, g in blocks:
                    last = nc.tensor.matmul(bank[Q * g:Q * g + rows, 0:n], state[:, k, :], w[:, k, g, :],
                                            start=(k == 0), stop=(k == J - 1), skip_group_check=True)
                return last

            def part(counts, u):
                first = sum(n for v, n in counts.items() if v < u)
                n = counts.get(u, 0)
                return BLOCKS[first:first + n], n and first == 0, n and first + n == len(BLOCKS)

            def chunk_products(c, u, behind, ahead):
                blocks, begins, ends = part(Y_PRODUCTS, u)
                if behind and blocks:
                    if begins:
                        eng.wait_ge(h0_last_ready, c)
                    last = product(wy, h0_last, bank_y, blocks)
                    if ends:
                        last.then_inc(y_mm, 1)
                blocks, begins, ends = part(P0_PRODUCTS, u)
                if ahead and blocks:
                    if begins:
                        eng.wait_ge(x_in_loaded, (c + 2) * 16)
                    last = product(wx0, x_in, bank_p0, blocks)
                    if ends:
                        last.then_inc(p0_mm, 1)
                blocks, begins, ends = part(P1_PRODUCTS, u)
                if behind and blocks:
                    if begins:
                        eng.wait_ge(x1_ready, c)
                    last = product(wx1, x1, bank_p1, blocks)
                    if ends:
                        last.then_inc(p1_mm, 1)

            def iteration(c, layer0, layer1, behind, ahead):
                for there in weights_in[1:3] if not behind else weights_in[3:] if not layer1 else ():
                    eng.wait_ge(there, 16)
                for u in range(TS):
                    if layer0:
                        eng.wait_ge(h0_done, c * TS + (u + 1))
                        product(wrz, h0, bank_rz, BLOCKS).then_inc(rz_mm, 1)
                    chunk_products(c, u, behind, ahead)
                    if layer1:
                        eng.wait_ge(h1_done, (c - 2) * TS + (u + 1))
                        product(wfow, h1, bank_fow, BLOCKS[:FOW_FIRST])
                    if layer0:
                        eng.wait_ge(rh_done, c * TS + (u + 1))
                        product(wh, rh, bank_h, BLOCKS).then_inc(h_mm, 1)
                    if layer1:
                        product(wfow, h1, bank_fow, BLOCKS[FOW_FIRST:]).then_inc(fow_mm, 1)

            eng.wait_ge(weights_in[0], 16)
            eng.wait_ge(x_in_loaded, 16)
            product(wx0, x_in, bank_p0, BLOCKS).then_inc(p0_mm, 1)
            eng.wait_ge(banks_cleared, 3)
            iterations(eng, iteration)

        @block.scalar
        def _(eng):
            def iteration(c, layer0, layer1, behind, ahead):
                for u in range(TS):
                    if layer0:
                        step = c * TS + (u + 1)
                        eng.wait_ge(r_summed, step)
                        nc.scalar.activation(r[:], r_pre[:], ACT.Sigmoid).then_inc(r_done, 1)
                        eng.wait_ge(z_summed, step)
                        nc.scalar.activation(z[:], z_pre[:], ACT.Sigmoid).then_inc(z_done, 1)
                        eng.wait_ge(h_summed, step)
                        nc.scalar.activation(cand0[:], h_pre[:], ACT.Tanh).then_inc(cand0_done, 1)
                        eng.wait_ge(h0_done, step + 1)
                        nc.scalar.activation(columns(h0_seq, u), h0[:], ACT.Copy).then_inc(h0_kept, 1)
                        if u == TS - 1:
                            eng.wait_ge(h0_kept, step + 1)
                            nc.scalar.activation(h0_last[:], h0_seq[:], ACT.Copy).then_inc(h0_last_ready, 1)
                    if layer1:
                        step = (c - 2) * TS + (u + 1)
                        eng.wait_ge(f_summed, step)
                        nc.scalar.activation(f[:], f_pre[:], ACT.Sigmoid).then_inc(f_done, 1)
                        eng.wait_ge(o_summed, step)
                        nc.scalar.activation(o[:], o_pre[:], ACT.Sigmoid).then_inc(o_done, 1)
                        eng.wait_ge(mem_done, step)
                        nc.scalar.activation(cand1[:], mem[:], ACT.Tanh).then_inc(cand1_done, 1)

            eng.sem_inc(h0_kept, 1)
            iterations(eng, iteration)

        @block.vector
        def _(eng):
            def flat(t):
                return t.rearrange("p j c -> p (j c)")

            def turn(to, bank, first, count):
                return nc.vector.transpose(flat(to[:, first:first + count, :]), bank[:, first * Q:(first + count) * Q])

            def new_share(to, gate, candidate):
                return nc.vector.scalar_tensor_tensor(out=to[:], in0=gate[:], scalar=1.0, in1=candidate[:],
                                                      op0=ALU.subtract, op1=ALU.mult)

            def set_up():
                for bank in (bank_rz, bank_h, bank_fow):
                    nc.vector.memset(bank[:], 0.0).then_inc(banks_cleared, 1)
                eng.wait_ge(consts_in, 32)
                nc.vector.tensor_copy(h0[:], h_first[:]).then_inc(h0_done, 1)
                nc.vector.tensor_copy(h1[:], h_first[:]).then_inc(h1_done, 1)
                nc.vector.tensor_tensor(gate_bias0[:], biases[:, 0:3, :], biases[:, 3:6, :], ALU.add).then_inc(biases_made, 1)
                for to, of in ((chunk_bias_y, biases[:, 6, :]), (hidden_bias, biases[:, 10, :]),
                               (chunk_bias1, biases[:, 7:10, :].rearrange("p m j -> p (m j)"))):
                    nc.vector.tensor_copy(to[:], of.unsqueeze(2).to_broadcast(list(to.shape))).then_inc(biases_made, 1)
                eng.wait_ge(biases_made, 4)
                of = gate_bias0[:].rearrange("p m j -> p (m j)")
                nc.vector.tensor_copy(chunk_bias0[:], of.unsqueeze(2).to_broadcast([P, 3 * J, Q])).then_inc(biases_made, 1)

            def chunk_turns(c, u, behind, ahead):
                if behind and u == Y_TURN:
                    eng.wait_ge(y_mm, c)
                    turn(y_t, bank_y, 0, J).then_inc(y_turned, 1)
                if ahead and u == P0_TURN:
                    eng.wait_ge(p0_mm, c + 2)
                    turn(next0, bank_p0, 0, 3 * J).then_inc(p0_turned, 1)
                if behind and u == P1_TURN:
                    eng.wait_ge(p1_mm, c)
                    turn(next1, bank_p1, 0, 3 * J).then_inc(p1_turned, 1)

            def iteration(c, layer0, layer1, behind, ahead):
                for u in range(TS):
                    if layer0:
                        step = c * TS + (u + 1)
                        eng.wait_ge(rz_mm, step)
                        turn(rz_t, bank_rz, 0, J).then_inc(r_turned, 1)
                        eng.wait_ge(r_turned, step)
                        if u == 0:
                            eng.wait_ge(proj0_ready, c + 1)
                        nc.vector.tensor_tensor(r_pre[:], turned(rz_t, 0, J), columns(proj0, u), ALU.add).then_inc(r_summed, 1)
                        turn(rz_t, bank_rz, J, J).then_inc(z_turned, 1)
                        eng.wait_ge(r_done, step)
                        nc.vector.tensor_tensor(rh[:], r[:], h0[:], ALU.mult).then_inc(rh_done, 1)
                        eng.wait_ge(z_turned, step)
                        nc.vector.tensor_tensor(z_pre[:], turned(rz_t, J, J), columns(proj0, u, J), ALU.add).then_inc(z_summed, 1)
                        eng.wait_ge(z_done, step)
                        eng.wait_ge(h0_kept, step)
                        nc.vector.tensor_tensor(kept0[:], z[:], h0[:], ALU.mult)
                    chunk_turns(c, u, behind, ahead)
                    if layer0:
                        eng.wait_ge(h_mm, step)
                        turn(h_t, bank_h, 0, J).then_inc(h_turned, 1)
                        eng.wait_ge(h_turned, step)
                        nc.vector.tensor_tensor(h_pre[:], turned(h_t, 0, J), columns(proj0, u, 2 * J), ALU.add).then_inc(h_summed, 1)
                        eng.wait_ge(cand0_done, step)
                        new_share(new0, z, cand0).then_inc(new0_done, 1)
                        eng.wait_ge(new0_done, step)
                        nc.vector.tensor_tensor(h0[:], kept0[:], new0[:], ALU.subtract).then_inc(h0_done, 1)
                    if layer1:
                        step = (c - 2) * TS + (u + 1)
                        eng.wait_ge(fow_mm, step)
                        turn(fow_t, bank_fow, 0, J).then_inc(f_turned, 1)
                        turn(fow_t, bank_fow, 2 * J, J).then_inc(w_turned, 1)
                        eng.wait_ge(f_turned, step)
                        if u == 0:
                            eng.wait_ge(proj1_ready, c - 1)
                        nc.vector.tensor_tensor(f_pre[:], turned(fow_t, 0, J), columns(proj1, u), ALU.add).then_inc(f_summed, 1)
                        eng.wait_ge(w_turned, step)
                        nc.vector.tensor_tensor(hid[:], turned(fow_t, 2 * J, J), hidden_bias[:], ALU.add).then_inc(hid_done, 1)
                        turn(fow_t, bank_fow, J, J).then_inc(o_turned, 1)
                        eng.wait_ge(f_done, step)
                        eng.wait_ge(hid_done, step)
                        nc.vector.tensor_tensor(gated[:], f[:], hid[:], ALU.mult).then_inc(gated_done, 1)
                        eng.wait_ge(o_turned, step)
                        nc.vector.tensor_tensor(o_pre[:], turned(fow_t, J, J), columns(proj1, u, J), ALU.add).then_inc(o_summed, 1)
                        eng.wait_ge(gated_done, step)
                        nc.vector.tensor_tensor(mem[:], gated[:], columns(proj1, u, 2 * J), ALU.add).then_inc(mem_done, 1)
                        eng.wait_ge(o_done, step)
                        eng.wait_ge(result_done, step)
                        nc.vector.tensor_tensor(kept1[:], o[:], h1[:], ALU.mult).then_inc(kept1_done, 1)
                        eng.wait_ge(cand1_done, step)
                        new_share(new1, o, cand1).then_inc(new1_done, 1)
                        eng.wait_ge(new1_done, step)
                        eng.wait_ge(kept1_done, step)
                        nc.vector.tensor_tensor(h1[:], kept1[:], new1[:], ALU.subtract).then_inc(h1_done, 1)

            set_up()
            eng.wait_ge(p0_mm, 1)
            turn(next0, bank_p0, 0, 3 * J).then_inc(p0_turned, 1)
            iterations(eng, iteration)

        @block.gpsimd
        def _(eng):
            def fill_proj0(c):
                eng.wait_ge(p0_turned, c + 1)
                nc.gpsimd.tensor_tensor(proj0[:], next0[:], chunk_bias0[:], ALU.add).then_inc(proj0_ready, 1)

            def iteration(c, layer0, layer1, behind, ahead):
                for u in range(TS):
                    if layer0 and u == TS - 1:
                        eng.wait_ge(h_summed, (c + 1) * TS)
                        fill_proj0(c + 1)
                    if behind and u == X1_STEP:
                        eng.wait_ge(x_res_loaded, c * 16)
                        nc.gpsimd.tensor_tensor(y_res[:], x_res[:], chunk_bias_y[:], ALU.add).then_inc(y_res_done, 1)
                        eng.wait_ge(y_res_done, c)
                        eng.wait_ge(y_turned, c)
                        nc.gpsimd.tensor_tensor(x1[:], y_res[:], y_t[:], ALU.add).then_inc(x1_ready, 1)
                    if layer1:
                        if u == 0:
                            eng.wait_ge(result_free, (c - 1) * 16)
                            eng.wait_ge(x1_here_ready, c - 1)
                        eng.wait_ge(h1_done, (c - 2) * TS + (u + 2))
                        nc.gpsimd.tensor_tensor(columns(result, u), columns(x1_here, u), h1[:], ALU.add).then_inc(result_done, 1)
                if behind:
                    eng.wait_ge(p1_turned, c)
                    nc.gpsimd.tensor_tensor(proj1[:], next1[:], chunk_bias1[:], ALU.add).then_inc(proj1_ready, 1)
                    if layer1:
                        eng.wait_ge(result_done, (c - 1) * TS + 1)
                    nc.gpsimd.tensor_tensor(x1_here[:], y_res[:], y_t[:], ALU.add).then_inc(x1_here_ready, 1)

            eng.sem_inc(result_done, 1)
            eng.wait_ge(biases_made, 5)
            fill_proj0(0)
            iterations(eng, iteration)


TS = 16


def kernel(x, cond_1024, L0_cond_Wxz, L0_cond_bxz, L0_cond_Whz, L0_cond_bhz, L0_cond_Wxr, L0_cond_bxr,
           L0_cond_Whr, L0_cond_bhr, L0_cond_Wxh, L0_cond_bxh, L0_cond_Whh, L0_cond_bhh, L0_cond_Whq,
           L0_cond_bhq, L1_cond_w_W, L1_cond_w_b, L1_cond_wx_W, L1_cond_wx_b, L1_cond_wh_W, L1_cond_wh_b):
    import concourse.bacc as bacc
    from concourse.bass_utils import run_bass_kernel_spmd

    x = np.asarray(x)
    Bt, T, C = x.shape
    J = C // P

    def features(a, axis):
        a = np.moveaxis(np.asarray(a), axis, 0)
        rest = a.shape[1:]
        a = a.reshape(G, J, Q, *rest).swapaxes(1, 2).reshape(P, J, *rest)
        return a

    def streamed(*mats):
        rows = [features(m, 0).reshape(P, J, G, P) for m in mats]
        return np.ascontiguousarray(np.concatenate(rows, axis=3))

    w_W, w_b = np.asarray(L1_cond_w_W), np.asarray(L1_cond_w_b)
    t = [np.asarray(m).T for m in (L0_cond_Whr, L0_cond_Whz, L0_cond_Whh, L0_cond_Wxr, L0_cond_Wxz, L0_cond_Wxh, L0_cond_Whq)]
    bias = [L0_cond_bxr, L0_cond_bxz, L0_cond_bxh, L0_cond_bhr, L0_cond_bhz, L0_cond_bhh, L0_cond_bhq,
            w_b[:C], w_b[C:], L1_cond_wx_b, L1_cond_wh_b]
    arrays = {
        "x_t": np.ascontiguousarray(features(x, 2).reshape(P, J, Bt, T // TS, TS).transpose(3, 0, 1, 4, 2)),
        "h_init": np.ascontiguousarray(features(cond_1024, 1)),
        "w_x0": streamed(t[3], t[4], t[5]),
        "w_rz": streamed(t[0], t[1]),
        "w_h": streamed(t[2]),
        "w_y": streamed(t[6]),
        "w_x1": streamed(w_W[:C, :C], w_W[:C, C:], np.asarray(L1_cond_wx_W)),
        "w_fow": streamed(w_W[C:, :C], w_W[C:, C:], np.asarray(L1_cond_wh_W)),
        "bias": np.ascontiguousarray(np.stack([features(b, 0) for b in bias], axis=1)),
    }
    nc = bacc.Bacc("TRN2", target_bir_lowering=False, num_devices=1)
    args = [nc.dram_tensor(n, a.shape, mybir.dt.from_np(a.dtype), kind="ExternalInput").ap() for n, a in arrays.items()]
    out = nc.dram_tensor("out_t", arrays["x_t"].shape, mybir.dt.float32, kind="ExternalOutput").ap()
    gated_recurrences(nc, *args, out)
    r = run_bass_kernel_spmd(nc, [arrays], core_ids=[0])
    got = r.results[0]["out_t"]
    got = got.transpose(4, 0, 3, 1, 2).reshape(Bt, T, G, Q, J)
    return np.ascontiguousarray(got.transpose(0, 1, 2, 4, 3).reshape(Bt, T, C))
```
